# Optimizing a Trainium2 kernel written in Bass

```python
import numpy as np
import jax
import jax.numpy as jnp

def _softmax(x, axis=-1):
    return jax.nn.softmax(x, axis=axis)

def _gelu(x):
    return jax.nn.gelu(x, approximate=True)

def _silu(x):
    return jax.nn.silu(x)

def _sigmoid(x):
    return jax.nn.sigmoid(x)

def _layernorm(x, axis=-1, eps=1e-05):
    m = jnp.mean(x, axis=axis, keepdims=True)
    v = jnp.var(x, axis=axis, keepdims=True)
    return (x - m) / jnp.sqrt(v + eps)

def _scatter_add(tgt, idx, src, axis=0):
    return tgt.at[idx].add(src)

def _segment_sum(src, seg, n):
    return jax.ops.segment_sum(src, seg, n)
kernel_name = 'mk_gnn_resnorm_d2_gnn_r32_54852b'

def setup_inputs(seed: int=0):
    np.random.seed(seed)
    _w = jnp.asarray

    def _rec_inputs():
        import jax
        import jax.numpy as jnp
        _gk = jax.random.key(seed)
        x = -0.000202 + 1 * jax.random.normal(jax.random.fold_in(_gk, 1), (3125, 128), jnp.float32)
        src = jax.random.randint(jax.random.fold_in(_gk, 2), (100000,), 0, 3125, jnp.int32)
        dst = jax.random.randint(jax.random.fold_in(_gk, 3), (100000,), 0, 3125, jnp.int32)
        _o = jnp.argsort(dst, stable=True)
        src = src[_o]
        dst = dst[_o]
        edge_attr_64 = 0.000102155 + 1.00015 * jax.random.normal(jax.random.fold_in(_gk, 11), (100000, 64), jnp.float32)
        edge_weight = jax.random.uniform(jax.random.fold_in(_gk, 13), (100000,), jnp.float32, 0.0, 0.999999)
        return (x, src, dst, edge_attr_64, edge_weight)
    x, src, dst, edge_attr_64, edge_weight = _rec_inputs()

    def _L0_gnn_setup():
        import jax, jax.numpy as jnp
        import numpy as np
        N_NODES = 50000
        N_EDGES = 50000
        IN_DIM = 128
        HID_DIM = 128

        def _gcn_conv(x, row, col, ew, W, b, n_nodes):
            deg = jax.ops.segment_sum(ew, col, num_segments=n_nodes)
            dis = jnp.where(deg > 0, jax.lax.rsqrt(deg), 0.0)
            norm = dis[row] * ew * dis[col]
            h = x @ W
            msg = h[row] * norm[:, None]
            out = jax.ops.segment_sum(msg, col, num_segments=n_nodes)
            return out + b
        key = jax.random.key(seed)
        k1, k2, k3, k4, k5 = jax.random.split(key, 5)
        x = jax.random.normal(k1, (N_NODES, IN_DIM), dtype=jnp.float32)
        edge_index = jax.random.randint(k2, (2, N_EDGES), 0, N_NODES, dtype=jnp.int64)
        edge_weight = jax.random.uniform(k3, (N_EDGES,), dtype=jnp.float32)
        s1 = (6.0 / (IN_DIM + HID_DIM)) ** 0.5
        W1 = jax.random.uniform(k4, (IN_DIM, HID_DIM), minval=-s1, maxval=s1, dtype=jnp.float32)
        b1 = jnp.zeros((HID_DIM,), dtype=jnp.float32)
        s2 = (6.0 / (HID_DIM + HID_DIM)) ** 0.5
        W2 = jax.random.uniform(k5, (HID_DIM, HID_DIM), minval=-s2, maxval=s2, dtype=jnp.float32)
        b2 = jnp.zeros((HID_DIM,), dtype=jnp.float32)
        return {'x': x, 'edge_index': edge_index, 'edge_weight': edge_weight, 'W1': W1, 'b1': b1, 'W2': W2, 'b2': b2}
    _L0_gnn_all = _L0_gnn_setup()
    _L0_gnn_in = {k: v for k, v in _L0_gnn_all.items() if k in ('W1', 'b1', 'W2', 'b2')}
    del _L0_gnn_all

    def _L1_gnn_setup():
        import jax, jax.numpy as jnp
        import numpy as np
        N_NODES = 3125
        N_EDGES = 15625
        IN_CH = 128
        EDGE_CH = 64

        def _glorot(key, shape):
            fan_in, fan_out = (shape[0], shape[1])
            lim = (6.0 / (fan_in + fan_out)) ** 0.5
            return jax.random.uniform(key, shape, jnp.float32, -lim, lim)
        key = jax.random.key(seed)
        ks = jax.random.split(key, 14)
        x = jax.random.normal(ks[0], (N_NODES, IN_CH), jnp.float32)
        edge_index = jax.random.randint(ks[1], (2, N_EDGES), 0, N_NODES, jnp.int64)
        edge_attr = jax.random.normal(ks[2], (N_EDGES, EDGE_CH), jnp.float32)
        timestamps = jax.random.uniform(ks[3], (N_EDGES,), jnp.float32)
        We1 = _glorot(ks[4], (EDGE_CH, 2 * EDGE_CH))
        be1 = jnp.zeros((2 * EDGE_CH,), jnp.float32)
        We2 = _glorot(ks[5], (2 * EDGE_CH, IN_CH))
        be2 = jnp.zeros((IN_CH,), jnp.float32)
        Wt = _glorot(ks[6], (1, IN_CH))
        bt = jnp.zeros((IN_CH,), jnp.float32)
        Wn1 = _glorot(ks[7], (2 * IN_CH, IN_CH))
        bn1 = jnp.zeros((IN_CH,), jnp.float32)
        Wn2 = _glorot(ks[8], (IN_CH, IN_CH))
        bn2 = jnp.zeros((IN_CH,), jnp.float32)
        return {'x': x, 'edge_index': edge_index, 'edge_attr': edge_attr, 'timestamps': timestamps, 'We1': We1, 'be1': be1, 'We2': We2, 'be2': be2, 'Wt': Wt, 'bt': bt, 'Wn1': Wn1, 'bn1': bn1, 'Wn2': Wn2, 'bn2': bn2}
    _L1_gnn_all = _L1_gnn_setup()
    _L1_gnn_in = {k: v for k, v in _L1_gnn_all.items() if k in ('We1', 'be1', 'We2', 'be2', 'Wt', 'bt', 'Wn1', 'bn1', 'Wn2', 'bn2')}
    del _L1_gnn_all
    return {'x': x, 'src': src, 'dst': dst, 'edge_attr_64': edge_attr_64, 'edge_weight': edge_weight, 'L0_gnn_W1': _L0_gnn_in['W1'], 'L0_gnn_b1': _L0_gnn_in['b1'], 'L0_gnn_W2': _L0_gnn_in['W2'], 'L0_gnn_b2': _L0_gnn_in['b2'], 'L1_gnn_We1': _L1_gnn_in['We1'], 'L1_gnn_be1': _L1_gnn_in['be1'], 'L1_gnn_We2': _L1_gnn_in['We2'], 'L1_gnn_be2': _L1_gnn_in['be2'], 'L1_gnn_Wt': _L1_gnn_in['Wt'], 'L1_gnn_bt': _L1_gnn_in['bt'], 'L1_gnn_Wn1': _L1_gnn_in['Wn1'], 'L1_gnn_bn1': _L1_gnn_in['bn1'], 'L1_gnn_Wn2': _L1_gnn_in['Wn2'], 'L1_gnn_bn2': _L1_gnn_in['bn2']}

def reference(x, src, dst, edge_attr_64, edge_weight, L0_gnn_W1, L0_gnn_b1, L0_gnn_W2, L0_gnn_b2, L1_gnn_We1, L1_gnn_be1, L1_gnn_We2, L1_gnn_be2, L1_gnn_Wt, L1_gnn_bt, L1_gnn_Wn1, L1_gnn_bn1, L1_gnn_Wn2, L1_gnn_bn2):
    import jax
    import jax.numpy as jnp

    def _L0_gnn_ref(x, edge_index, edge_weight, W1, b1, W2, b2):
        import jax, jax.numpy as jnp
        import numpy as np
        N_NODES = 50000
        N_EDGES = 50000
        IN_DIM = 128
        HID_DIM = 128

        def _gcn_conv(x, row, col, ew, W, b, n_nodes):
            deg = jax.ops.segment_sum(ew, col, num_segments=n_nodes)
            dis = jnp.where(deg > 0, jax.lax.rsqrt(deg), 0.0)
            norm = dis[row] * ew * dis[col]
            h = x @ W
            msg = h[row] * norm[:, None]
            out = jax.ops.segment_sum(msg, col, num_segments=n_nodes)
            return out + b
        n_nodes = x.shape[0]
        loop = jnp.arange(n_nodes, dtype=edge_index.dtype)
        row = jnp.concatenate([edge_index[0], loop])
        col = jnp.concatenate([edge_index[1], loop])
        ew = jnp.concatenate([edge_weight, jnp.ones((n_nodes,), dtype=edge_weight.dtype)])
        h = jax.nn.relu(_gcn_conv(x, row, col, ew, W1, b1, n_nodes))
        return _gcn_conv(h, row, col, ew, W2, b2, n_nodes)

    def _L1_gnn_ref(x, edge_index, edge_attr, timestamps, We1, be1, We2, be2, Wt, bt, Wn1, bn1, Wn2, bn2):
        import jax, jax.numpy as jnp
        import numpy as np
        N_NODES = 3125
        N_EDGES = 15625
        IN_CH = 128
        EDGE_CH = 64

        def _glorot(key, shape):
            fan_in, fan_out = (shape[0], shape[1])
            lim = (6.0 / (fan_in + fan_out)) ** 0.5
            return jax.random.uniform(key, shape, jnp.float32, -lim, lim)
        ts = timestamps[:, None]
        ef = jax.nn.relu(edge_attr @ We1 + be1) @ We2 + be2
        tw = jax.nn.sigmoid(ts @ Wt + bt)
        ef = ef * tw
        row, col = (edge_index[0], edge_index[1])
        combined = jnp.concatenate([x[row], ef], axis=1)
        msg = jax.nn.relu(combined @ Wn1 + bn1) @ Wn2 + bn2
        out = jax.ops.segment_sum(msg, col, num_segments=x.shape[0])
        return out + x
    edge_index = jnp.stack([src, dst])
    x = _layernorm(x + _L0_gnn_ref(x, edge_index, edge_weight, L0_gnn_W1, L0_gnn_b1, L0_gnn_W2, L0_gnn_b2), axis=-1)
    x = _layernorm(x + _L1_gnn_ref(x, edge_index, edge_attr_64, edge_weight, L1_gnn_We1, L1_gnn_be1, L1_gnn_We2, L1_gnn_be2, L1_gnn_Wt, L1_gnn_bt, L1_gnn_Wn1, L1_gnn_bn1, L1_gnn_Wn2, L1_gnn_bn2), axis=-1)
    return x

_drawn_inputs = setup_inputs


def setup_inputs(seed=0):
    import zlib

    import numpy as np

    out = dict(_drawn_inputs(seed))
    spreads = {'L0_gnn_b1': (0.0, 0.1),
     'L0_gnn_b2': (0.0, 0.1),
     'L1_gnn_be1': (0.0, 0.374),
     'L1_gnn_be2': (0.0, 0.1),
     'L1_gnn_bt': (0.0, 0.763),
     'L1_gnn_bn1': (0.0, 0.1),
     'L1_gnn_bn2': (0.0, 0.1)}
    factors = {'edge_weight': 8.0, 'L0_gnn_W1': 3.805, 'L1_gnn_Wt': 8.0}
    for name, (base, spread) in spreads.items():
        noise = np.random.default_rng([zlib.crc32(name.encode()), seed]).standard_normal(out[name].shape)
        drawn = base * np.exp(spread * noise) if base else spread * noise
        out[name] = jnp.asarray(drawn.astype(out[name].dtype))
    for name, factor in factors.items():
        out[name] = (out[name] * factor).astype(out[name].dtype)
    return out
```

```python
from contextlib import ExitStack

import concourse.bass as bass
from concourse import mybir

F32 = mybir.dt.float32
I32 = mybir.dt.int32
U32 = mybir.dt.uint32
ALU = mybir.AluOpType
ACT = mybir.ActivationFunctionType
AX = mybir.AxisListType

P = 128
N = 3125
NP = 125
NT = N // NP
C = 128
EC = 64
E = 100000
GT = 8
GE = GT * P
NG = -(-E // GE)
TILES = NG * GT
EP = NG * GE
WIN = 48
ACCW = 3200
LASTWIN = ACCW - WIN - 16
CH = 4
CE = CH * P
NC = NG * 2
EPS = 1e-5
NCHUNK = 500
NODE_CHUNKS = [(a, min(NCHUNK, N - a)) for a in range(0, N, NCHUNK)]
assert NT * NP == N and NG % 2 == 0


def build(nc, x, xt, src, dst, ew, ew_row, ea_t, w1, b1, w2, b2, we1, be1, we2, be2, wt, bt,
          wn1, bn1, wn2, bn2, out):
    with ExitStack() as ctx:
        def sb(name, shape, dt=F32):
            return ctx.enter_context(nc.sbuf_tensor(name, shape, dt))

        def sem(name):
            return ctx.enter_context(nc.semaphore(name))

        table1 = nc.dram_tensor("table1", (N, C), F32).ap()
        table2 = nc.dram_tensor("table2", (N, C), F32).ap()
        table3 = nc.dram_tensor("table3", (N, C), F32).ap()

        def node_rows(t):
            return t.rearrange("(t p) c -> p t c", p=NP)

        w1_sb = sb("w1_sb", [C, C])
        w2_sb = sb("w2_sb", [C, C])
        we1_sb = sb("we1_sb", [EC, C])
        we2_sb = sb("we2_sb", [C, C])
        wn1a_sb = sb("wn1a_sb", [C, C])
        wn1b_sb = sb("wn1b_sb", [C, C])
        wn2_sb = sb("wn2_sb", [C, C])
        b1_col = sb("b1_col", [C, 1])
        be1_col = sb("be1_col", [C, 1])
        be2_col = sb("be2_col", [C, 1])
        wt_col = sb("wt_col", [C, 1])
        bt_col = sb("bt_col", [C, 1])
        b2_row = sb("b2_row", [1, C])
        bn1_row = sb("bn1_row", [1, C])
        bn2_row = sb("bn2_row", [1, C])
        x_rows = sb("x_rows", [NP, NT, C])
        x1_rows = sb("x1_rows", [NP, NT, C])
        scr_rows = sb("scr_rows", [NP, NT, C])
        xT = sb("xT", [C, N])
        h1s = sb("h1s", [C, N])
        acc = sb("acc", [C, ACCW])
        degcnt = sb("degcnt", [P, 2, ACCW])
        dis = sb("dis", [P, N])
        dis_col = sb("dis_col", [NP, NT])
        stats = sb("stats", [NP, NT, 6])
        mv = sb("mv", [NP, NT, 2])
        rstd = sb("rstd", [NP, NT])
        sdev = sb("sdev", [NP, NT])
        dst_i = sb("dst_i", [P, TILES], I32)
        dst_f = sb("dst_f", [P, TILES])
        dst_rel = sb("dst_rel", [P, TILES])
        ew_sb = sb("ew_sb", [P, TILES])
        lo = sb("lo", [P, NG])
        hi = sb("hi", [P, NG])
        lo_now = sb("lo_now", [P, NG])
        win_f = sb("win_f", [1, NG])
        win_i = sb("win_i", [1, NG], I32)
        diag = sb("diag", [NG, 2, NG])
        lohi_g = sb("lohi_g", [NG, 2])
        spans_f = sb("spans_f", [1, 2])
        spans_i = sb("spans_i", [1, 1], I32)
        ident_i = sb("ident_i", [P, P], I32)
        ident = sb("ident", [P, P])
        ones = sb("ones", [P, P])
        iota_i = sb("iota_i", [P, WIN], I32)
        iota = sb("iota", [P, WIN])
        carrier = sb("carrier", [P, 1])
        pool_ones = sb("pool_ones", [P, 1])
        eps_col = sb("eps_col", [P, 1])
        idx = sb("idx", [P, 2, GT], U32)
        got = sb("got", [P, 2, GT, C])
        onehot = sb("onehot", [P, 2, GT, 2, WIN])
        ea = sb("ea", [EC, 2, GE])
        tsb = sb("tsb", [P, 2, GE])
        hid = sb("hid", [C, 2, CE])
        tw = sb("tw", [C, 2, CE])
        ef = sb("ef", [C, 2, CE])
        pre = sb("pre", [P, 2, CE])
        msg = sb("msg", [P, 2, CE])

        banks = [ctx.enter_context(nc.psum_tensor(f"bank{i}", [P, 512], F32)) for i in range(8)]

        loaded = sem("loaded")
        loaded2 = sem("loaded2")
        made = sem("made")
        chain = sem("chain")
        turned = sem("turned")
        spans_ready = sem("spans_ready")

        small = [(w1_sb, w1), (w2_sb, w2), (we1_sb, we1), (we2_sb, we2), (wn1a_sb, wn1[0:C, :]),
                 (wn1b_sb, wn1[C:2 * C, :]), (wn2_sb, wn2)]
        cols = [(b1_col, b1), (be1_col, be1), (be2_col, be2), (bt_col, bt)]
        rows = [(b2_row, b2), (bn1_row, bn1), (bn2_row, bn2)]
        with nc.Block() as block:
            @block.sync
            def _(sp):
                sp.dma_start(dst_i[:, :], dst).then_inc(loaded, 16)
                sp.dma_start(ew_sb[:, :], ew).then_inc(loaded2, 16)
                sp.dma_start(x_rows[:, :, :], node_rows(x)).then_inc(loaded2, 16)
                sp.dma_start(xT[:, :], xt).then_inc(loaded2, 16)
                for a, b in small:
                    sp.dma_start(a[:, :], b).then_inc(loaded2, 16)
                for a, b in cols:
                    sp.dma_start(a[:, :], b.rearrange("(p a) -> p a", a=1)).then_inc(loaded2, 16)
                sp.dma_start(wt_col[:, :], wt.rearrange("a p -> p a")).then_inc(loaded2, 16)
                for a, b in rows:
                    sp.dma_start(a[:, :], b.rearrange("(a p) -> a p", a=1)).then_inc(loaded2, 16)
                sp.wait_ge(loaded2, 16 * (4 + len(small) + len(cols) + len(rows)))

            @block.gpsimd
            def _(pool):
                pool.iota(ident_i[:, :], pattern=[[1, P]], base=0, channel_multiplier=-1).then_inc(made, 1)
                pool.memset(pool_ones[:, :], 1.0).then_inc(made, 1)
                pool.iota(iota_i[:, :], pattern=[[1, WIN]], base=0, channel_multiplier=0).then_inc(made, 1)

            @block.vector
            def _(dve):
                done = 0

                def step(ins):
                    nonlocal done
                    done += 1
                    ins.then_inc(chain, 1)

                def settle():
                    dve.wait_ge(chain, done)

                step(dve.memset(ones[:, :], 1.0))
                step(dve.memset(degcnt[:, :, :], 0.0))
                step(dve.memset(acc[:, :], 0.0))
                step(dve.memset(eps_col[:, :], EPS))
                dve.wait_ge(made, 3)
                step(dve.tensor_scalar(ident[:, :], ident_i[:, :], 0.0, None, ALU.is_equal))
                step(dve.tensor_copy(iota[:, :], iota_i[:, :]))
                dve.wait_ge(loaded, 16)
                step(dve.tensor_copy(dst_f[:, :], dst_i[:, :]))
                settle()
                by_group = dst_f[:, :].rearrange("p (g t) -> p g t", t=GT)
                step(dve.tensor_reduce(lo[:, :], by_group, AX.X, ALU.min))
                step(dve.tensor_reduce(hi[:, :], by_group, AX.X, ALU.max))
                settle()
                dve.wait_ge(turned, 2)
                step(dve.tensor_reduce(lohi_g[:, 0:1], banks[0][0:NG, 0:P], AX.X, ALU.min))
                step(dve.tensor_reduce(lohi_g[:, 1:2], banks[1][0:NG, 0:P], AX.X, ALU.max))
                settle()
                for k in range(2):
                    step(dve.tensor_scalar(diag[:, k, :], ident[0:NG, 0:NG], lohi_g[:, k:k + 1], None, ALU.mult))
                settle()
                dve.wait_ge(turned, 3)
                step(dve.tensor_copy(lo[:, :], banks[2][:, 0:NG]))
                step(dve.tensor_copy(hi[:, :], banks[2][:, NG:2 * NG]))
                settle()
                step(dve.tensor_tensor(hi[:, :], hi[:, :], lo[:, :], ALU.subtract))
                settle()
                step(dve.tensor_reduce(spans_f[:, 0:1], hi[0:1, :], AX.X, ALU.max))
                settle()
                step(dve.tensor_scalar(spans_f[:, 1:2], spans_f[:, 0:1], 1.0 / WIN, 1.0 - (WIN - 1) / (2.0 * WIN),
                                       ALU.mult, ALU.add))
                settle()
                step(dve.tensor_copy(spans_i[:, :], spans_f[:, 1:2]))
                settle()

            @block.tensor
            def _(pe):
                pe.wait_ge(chain, 9)
                pe.transpose(banks[0][0:NG, 0:P], lo[:, :], ident[:, :]).then_inc(turned, 1)
                pe.transpose(banks[1][0:NG, 0:P], hi[:, :], ident[:, :]).then_inc(turned, 1)
                pe.wait_ge(chain, 13)
                pe.matmul(banks[2][:, 0:2 * NG], ones[0:NG, :], diag[:, :, :],
                          start=True, stop=True).then_inc(turned, 1)

        spans = nc.values_load(spans_i[0:1, 0:1], min_val=1, max_val=-(-(N + 1) // WIN))

        def open_pass(dve, p, st, own):
            dve.tensor_tensor(dst_rel[:, :].rearrange("q (g t) -> q g t", t=GT),
                              dst_f[:, :].rearrange("q (g t) -> q g t", t=GT),
                              lo_now[:, :].unsqueeze(2).broadcast_to([P, NG, GT]), ALU.subtract).then_inc(own, 1)
            dve.tensor_scalar(win_f[:, :], lo_now[0:1, :], float(LASTWIN), None, ALU.min).then_inc(own, 1)
            dve.wait_ge(own, p * 4 + 3)
            dve.tensor_copy(win_i[:, :], win_f[:, :]).then_inc(own, 1)
            dve.tensor_scalar(lo_now[:, :], lo_now[:, :], float(WIN), None, ALU.add).then_inc(own, 1)
            dve.wait_ge(own, p * 4 + 5)

        def one_hot(dve, slot, g, place):
            return dve.tensor_tensor(onehot[:, slot, :, place, :], iota[:, :].unsqueeze(1).broadcast_to([P, GT, WIN]),
                                     dst_rel[:, bass.ds(g * GT, GT)].unsqueeze(2).broadcast_to([P, GT, WIN]),
                                     ALU.is_equal)

        def weigh(dve, slot, g):
            return dve.tensor_tensor(onehot[:, slot, :, 0, :], onehot[:, slot, :, 1, :],
                                     ew_sb[:, bass.ds(g * GT, GT)].unsqueeze(2).broadcast_to([P, GT, WIN]),
                                     ALU.mult)

        def degree_stage():
            opened = sem("deg_opened")
            own = sem("deg_own")
            hot = sem("deg_hot")
            weights_ready = sem("deg_weights")
            summed = sem("deg_summed")
            added = sem("deg_added")
            with nc.Block() as block:
                @block.vector
                def _(dve):
                    dve.tensor_copy(lo_now[:, :], lo[:, :]).then_inc(own, 1)
                    with dve.Fori(0, spans) as p:
                        dve.wait_ge(own, p * 4 + 1)
                        open_pass(dve, p, 0, own)
                        dve.nop().then_inc(opened, 1)

                        def body(i, k, first):
                            g = i * 2 + k
                            n = p * NG + g
                            if not first:
                                dve.wait_ge(summed, n - 1)
                            one_hot(dve, k, g, 1).then_inc(hot, 1)
                            dve.wait_ge(hot, n + 1)
                            weigh(dve, k, g).then_inc(weights_ready, 1)
                            if not (first and k == 0):
                                add(g - 1, n - 1, 1 - k, first and k == 1)

                        def add(g, n, k, very_first):
                            win = dve.value_load(win_i[0:1, bass.ds(g, 1)], min_val=0, max_val=LASTWIN)
                            dve.wait_ge(summed, n + 1)
                            if not very_first:
                                dve.wait_ge(added, n)
                            a = degcnt[:, :, bass.ds(win, WIN)]
                            dve.tensor_tensor(a, a, banks[k][:, 0:2 * WIN].rearrange("q (a w) -> q a w", a=2),
                                              ALU.add).then_inc(added, 1)

                        body(0, 0, True)
                        body(0, 1, True)
                        with dve.Fori(1, NG // 2) as i:
                            body(i, 0, False)
                            body(i, 1, False)
                        add(NG - 1, p * NG + NG - 1, 1, False)
                        dve.wait_ge(added, p * NG + NG)

                @block.tensor
                def _(pe):
                    with pe.Fori(0, spans) as p:
                        pe.wait_ge(opened, p + 1)

                        def body(i, k, first):
                            n = p * NG + i * 2 + k
                            pe.wait_ge(weights_ready, n + 1)
                            if not first:
                                pe.wait_ge(added, n - 1)
                            for t in range(GT):
                                last = pe.matmul(banks[k][:, 0:2 * WIN], ones[:, :], onehot[:, k, t, :, :],
                                                 start=(t == 0), stop=(t == GT - 1))
                            last.then_inc(summed, 1)

                        body(0, 0, True)
                        body(0, 1, True)
                        with pe.Fori(1, NG // 2) as i:
                            body(i, 0, False)
                            body(i, 1, False)

        def load_indices(sp, p, i, k, idx_ready):
            g = i * 2 + k
            sp.dma_start(idx[:, k, :], src[:, bass.ds(g * GT, GT)]).then_inc(idx_ready[k], 16)

        def gather(pool, p, i, k, table, idx_ready, landed, carried):
            pool.wait_ge(idx_ready[k], (p * (NG // 2) + i) * 16 + 16)
            pool.wait_ge(carried, p * NG + i * 2 + k + 1)
            pool.tensor_tensor(carrier[:, :], pool_ones[:, :], pool_ones[:, :], ALU.add).then_inc(carried, 1)
            for t in range(GT):
                pool.indirect_dma_start(got[:, k, t, :], None, table,
                                        bass.IndirectOffsetOnAxis(ap=idx[:, k, t:t + 1], axis=0)
                                        ).then_inc(landed[k][t], 16)

        def conv_stage(name, table):
            opened = sem(name + "_opened")
            own = sem(name + "_own")
            hot = sem(name + "_hot")
            weights_ready = sem(name + "_weights")
            summed = sem(name + "_summed")
            added = sem(name + "_added")
            idx_ready = [sem(f"{name}_idx{k}") for k in range(2)]
            carried = sem(name + "_carried")
            landed = [[sem(f"{name}_landed{k}_{t}") for t in range(GT)] for k in range(2)]
            with nc.Block() as block:
                @block.sync
                def _(sp):
                    with sp.Fori(0, spans) as p:
                        sp.wait_ge(opened, p + 1)
                        load_indices(sp, p, 0, 0, idx_ready)
                        load_indices(sp, p, 0, 1, idx_ready)
                        with sp.Fori(1, NG // 2) as i:
                            for k in range(2):
                                sp.wait_ge(summed, p * NG + i * 2 + k - 1)
                                load_indices(sp, p, i, k, idx_ready)

                @block.gpsimd
                def _(pool):
                    pool.memset(carrier[:, :], 0.0).then_inc(carried, 1)
                    with pool.Fori(0, spans) as p:
                        with pool.Fori(0, NG // 2) as i:
                            for k in range(2):
                                gather(pool, p, i, k, table, idx_ready, landed, carried)

                @block.vector
                def _(dve):
                    dve.tensor_copy(lo_now[:, :], lo[:, :]).then_inc(own, 1)
                    with dve.Fori(0, spans) as p:
                        dve.wait_ge(own, p * 4 + 1)
                        open_pass(dve, p, 0, own)
                        dve.nop().then_inc(opened, 1)

                        def body(i, k, first):
                            g = i * 2 + k
                            n = p * NG + g
                            if not first:
                                dve.wait_ge(summed, n - 1)
                            one_hot(dve, k, g, 1).then_inc(hot, 1)
                            dve.wait_ge(hot, n + 1)
                            weigh(dve, k, g).then_inc(weights_ready, 1)
                            if not (first and k == 0):
                                add(g - 1, n - 1, 1 - k, first and k == 1)

                        def add(g, n, k, very_first):
                            win = dve.value_load(win_i[0:1, bass.ds(g, 1)], min_val=0, max_val=LASTWIN)
                            dve.wait_ge(summed, n + 1)
                            if not very_first:
                                dve.wait_ge(added, n)
                            a = acc[:, bass.ds(win, WIN)]
                            dve.tensor_tensor(a, a, banks[k][:, 0:WIN], ALU.add).then_inc(added, 1)

                        body(0, 0, True)
                        body(0, 1, True)
                        with dve.Fori(1, NG // 2) as i:
                            body(i, 0, False)
                            body(i, 1, False)
                        add(NG - 1, p * NG + NG - 1, 1, False)
                        dve.wait_ge(added, p * NG + NG)

                @block.tensor
                def _(pe):
                    with pe.Fori(0, spans) as p:
                        pe.wait_ge(opened, p + 1)

                        def body(i, k, first):
                            n = p * NG + i * 2 + k
                            pe.wait_ge(weights_ready, n + 1)
                            if not first:
                                pe.wait_ge(added, n - 1)
                            for t in range(GT):
                                pe.wait_ge(landed[k][t], (p * (NG // 2) + i) * 16 + 16)
                                last = pe.matmul(banks[k][:, 0:WIN], got[:, k, t, :], onehot[:, k, t, 0, :],
                                                 start=(t == 0), stop=(t == GT - 1))
                            last.then_inc(summed, 1)

                        body(0, 0, True)
                        body(0, 1, True)
                        with pe.Fori(1, NG // 2) as i:
                            body(i, 0, False)
                            body(i, 1, False)

        def scale_stage():
            c = sem("dis_chain")
            rooted = sem("dis_rooted")
            turned1 = sem("dis_turned")
            table_made = sem("table1_made")
            stored = sem("table1_stored")
            with nc.Block() as block:
                @block.vector
                def _(dve):
                    deg = degcnt[:, 0, 0:N]
                    dve.tensor_scalar(deg, deg, 1.0, None, ALU.add).then_inc(c, 1)
                    dve.wait_ge(c, 1)
                    dve.tensor_scalar(dis[:, :], deg, 2.0 ** -100, None, ALU.max).then_inc(c, 1)
                    dve.wait_ge(rooted, 1)
                    dve.reciprocal(dis[:, :], dis[:, :]).then_inc(c, 1)
                    dve.wait_ge(c, 3)
                    dve.scalar_tensor_tensor(out=dis[:, :], in0=deg, scalar=0.0, in1=dis[:, :],
                                             op0=ALU.is_gt, op1=ALU.mult).then_inc(c, 1)
                    dve.wait_ge(turned1, 1)
                    dve.tensor_copy(dis_col[:, :], banks[0][0:NP, 0:NT]).then_inc(c, 1)
                    dve.wait_ge(c, 5)
                    dve.tensor_tensor(scr_rows[:, :, :], x_rows[:, :, :],
                                      dis_col[:, :].unsqueeze(2).broadcast_to([NP, NT, C]), ALU.mult).then_inc(table_made, 1)

                @block.scalar
                def _(act):
                    act.wait_ge(c, 2)
                    act.activation(dis[:, :], dis[:, :], ACT.Sqrt).then_inc(rooted, 1)

                @block.tensor
                def _(pe):
                    pe.wait_ge(c, 4)
                    for t in range(NT):
                        last = pe.matmul(banks[0][0:NP, t:t + 1], dis[0:1, t * NP:(t + 1) * NP], ones[0:1, 0:1],
                                         start=True, stop=True)
                    last.then_inc(turned1, 1)

                @block.sync
                def _(sp):
                    sp.wait_ge(table_made, 1)
                    sp.dma_start(node_rows(table1), scr_rows[:, :, :]).then_inc(stored, 16)
                    sp.wait_ge(stored, 16)

        def hidden_stage():
            c = sem("h1_chain")
            mm = sem("h1_mm")
            relued = sem("h1_relued")
            scaled = sem("h1_scaled")
            turned2 = sem("h1_turned")
            copied = sem("h1_copied")
            stored = sem("table2_stored")
            zeroed = sem("h1_zeroed")
            with nc.Block() as block:
                @block.vector
                def _(dve):
                    for j, (a, n) in enumerate(NODE_CHUNKS):
                        s = slice(a, a + n)
                        dve.tensor_tensor(h1s[:, s], xT[:, s], dis[:, s], ALU.mult).then_inc(c, 1)
                        dve.wait_ge(c, 3 * j + 1)
                        dve.tensor_tensor(h1s[:, s], h1s[:, s], acc[:, s], ALU.add).then_inc(c, 1)
                        dve.wait_ge(c, 3 * j + 2)
                        dve.tensor_tensor(acc[:, s], h1s[:, s], dis[:, s], ALU.mult).then_inc(c, 1)
                    for j, (a, n) in enumerate(NODE_CHUNKS):
                        s = slice(a, a + n)
                        dve.wait_ge(relued, j + 1)
                        dve.tensor_tensor(h1s[:, s], h1s[:, s], dis[:, s], ALU.mult).then_inc(scaled, 1)
                    dve.wait_ge(mm, len(NODE_CHUNKS))
                    dve.memset(acc[:, :], 0.0).then_inc(zeroed, 1)

                @block.tensor
                def _(pe):
                    for j, (a, n) in enumerate(NODE_CHUNKS):
                        pe.wait_ge(c, 3 * j + 3)
                        if j >= 4:
                            pe.wait_ge(relued, j - 3)
                        pe.matmul(banks[j % 4][:, 0:n], w1_sb[:, :], acc[:, a:a + n], start=True, stop=True).then_inc(mm, 1)
                    for t in range(NT):
                        pe.wait_ge(scaled, min((t * NP + NP - 1) // NCHUNK, len(NODE_CHUNKS) - 1) + 1)
                        if t >= 4:
                            pe.wait_ge(copied, t - 3)
                        pe.transpose(banks[4 + t % 4][0:NP, 0:C], h1s[:, t * NP:(t + 1) * NP], ident[:, :]).then_inc(turned2, 1)

                @block.scalar
                def _(act):
                    for j, (a, n) in enumerate(NODE_CHUNKS):
                        act.wait_ge(mm, j + 1)
                        act.activation(h1s[:, a:a + n], banks[j % 4][:, 0:n], ACT.Relu, bias=b1_col[:, 0:1]).then_inc(relued, 1)
                    for t in range(NT):
                        act.wait_ge(turned2, t + 1)
                        act.copy(scr_rows[:, t, :], banks[4 + t % 4][0:NP, 0:C]).then_inc(copied, 1)

                @block.sync
                def _(sp):
                    sp.wait_ge(copied, NT)
                    sp.dma_start(node_rows(table2), scr_rows[:, :, :]).then_inc(stored, 16)
                    sp.wait_ge(stored, 16)

        def layer_norm(dve, to, c, base, rooted):
            for t in range(NT):
                dve.bn_stats(stats[:, t, :], scr_rows[:, t, :]).then_inc(c, 1)
            dve.wait_ge(c, base + NT)
            for t in range(NT):
                last = dve.bn_aggr(mv[:, t, :], stats[:, t, :])
            last.then_inc(c, 1)
            dve.wait_ge(rooted, 1)
            dve.reciprocal(rstd[:, :], sdev[:, :]).then_inc(c, 1)
            dve.wait_ge(c, base + NT + 2)
            for t in range(NT):
                last = dve.tensor_scalar(to[:, t, :], scr_rows[:, t, :], mv[:, t, 0:1], rstd[:, t:t + 1],
                                         ALU.subtract, ALU.mult)
            last.then_inc(c, 1)

        def middle_stage():
            c = sem("x1_chain")
            mm = sem("x1_mm")
            summed = sem("x1_summed")
            rooted = sem("x1_rooted")
            turned3 = sem("x1_turned")
            columns = sem("x1_columns")
            mm3 = sem("t3_mm")
            copied = sem("t3_copied")
            stored = sem("table3_stored")
            with nc.Block() as block:
                @block.vector
                def _(dve):
                    for j, (a, n) in enumerate(NODE_CHUNKS):
                        s = slice(a, a + n)
                        dve.tensor_tensor(acc[:, s], h1s[:, s], acc[:, s], ALU.add).then_inc(c, 1)
                        dve.wait_ge(c, 2 * j + 1)
                        dve.tensor_tensor(acc[:, s], acc[:, s], dis[:, s], ALU.mult).then_inc(c, 1)
                    for t in range(NT):
                        dve.wait_ge(mm, t + 1)
                        dve.tensor_tensor(scr_rows[:, t, :], banks[t % 4][0:NP, 0:C], x_rows[:, t, :], ALU.add).then_inc(summed, 1)
                    dve.wait_ge(summed, NT)
                    layer_norm(dve, x1_rows, c, 2 * len(NODE_CHUNKS), rooted)
                    dve.memset(acc[:, :], 0.0).then_inc(c, 1)
                    for t in range(NT):
                        dve.wait_ge(mm3, t + 1)
                        dve.tensor_copy(scr_rows[:, t, :], banks[4 + t % 4][0:NP, 0:C]).then_inc(copied, 1)

                @block.tensor
                def _(pe):
                    for t in range(NT):
                        pe.wait_ge(c, 2 * min((t * NP + NP - 1) // NCHUNK, len(NODE_CHUNKS) - 1) + 2)
                        if t >= 4:
                            pe.wait_ge(summed, t - 3)
                        b = banks[t % 4][0:NP, 0:C]
                        pe.matmul(b, acc[:, t * NP:(t + 1) * NP], w2_sb[:, :], start=True, stop=False)
                        pe.matmul(b, ones[0:1, 0:NP], b2_row[:, :], start=False, stop=True).then_inc(mm, 1)
                    pe.wait_ge(c, 2 * len(NODE_CHUNKS) + NT + 3)
                    for t in range(NT + 1):
                        if t < NT:
                            if t >= 4:
                                pe.wait_ge(columns, t - 3)
                            pe.transpose(banks[t % 4][0:C, 0:NP], x1_rows[:, t, :], ident[0:NP, 0:NP]).then_inc(turned3, 1)
                        if t >= 1:
                            u = t - 1
                            pe.wait_ge(columns, u + 1)
                            if u >= 4:
                                pe.wait_ge(copied, u - 3)
                            b = banks[4 + u % 4][0:NP, 0:C]
                            pe.matmul(b, h1s[:, u * NP:(u + 1) * NP], wn1a_sb[:, :], start=True, stop=False)
                            pe.matmul(b, ones[0:1, 0:NP], bn1_row[:, :], start=False, stop=True).then_inc(mm3, 1)

                @block.scalar
                def _(act):
                    act.wait_ge(c, 2 * len(NODE_CHUNKS) + NT + 1)
                    act.activation(sdev[:, :], mv[:, :, 1], ACT.Sqrt, bias=eps_col[0:NP, 0:1]).then_inc(rooted, 1)
                    for t in range(NT):
                        act.wait_ge(turned3, t + 1)
                        act.copy(h1s[:, t * NP:(t + 1) * NP], banks[t % 4][0:C, 0:NP]).then_inc(columns, 1)

                @block.sync
                def _(sp):
                    sp.wait_ge(copied, NT)
                    sp.dma_start(node_rows(table3), scr_rows[:, :, :]).then_inc(stored, 16)
                    sp.wait_ge(stored, 16)

        def message_stage():
            opened = sem("msg_opened")
            own = sem("msg_own")
            hot = sem("msg_hot")
            idx_ready = [sem(f"msg_idx{k}") for k in range(2)]
            carried = sem("msg_carried")
            landed = [[sem(f"msg_landed{k}_{t}") for t in range(GT)] for k in range(2)]
            ea_ready = [sem(f"msg_ea{k}") for k in range(2)]
            ts_ready = [sem(f"msg_ts{k}") for k in range(2)]
            hid_mm = sem("hid_mm")
            hid_ready = sem("hid_ready")
            ef_mm = sem("ef_mm")
            tw_ready = sem("tw_ready")
            ef_ready = sem("ef_ready")
            pre_mm = sem("pre_mm")
            pre_ready = sem("pre_ready")
            msg_ready = sem("msg_ready")
            seg_mm = sem("seg_mm")
            added = sem("msg_added")
            LAST = NC
            LOOPS = NC // 4 - 1

            def steps(eng, p, step):
                for s in range(-1, 4):
                    step(s, p * NC + s, s % 4, s)
                with eng.Fori(1, LOOPS) as i:
                    for k in range(4):
                        step(None, p * NC + i * 4 + k, k, i * 4 + k)
                for s in range(4 * LOOPS, LAST + 2):
                    step(s, p * NC + s, s % 4, s)

            with nc.Block() as block:
                @block.sync
                def _(sp):
                    def load(p, g, k):
                        sp.dma_start(ea[:, k, :], ea_t[:, bass.ds(g * GE, GE)]).then_inc(ea_ready[k], 16)
                        sp.dma_start(tsb[:, k, :], ew_row[:, bass.ds(g * GE, GE)].broadcast_to([P, GE])).then_inc(ts_ready[k], 16)

                    with sp.Fori(0, spans) as p:
                        sp.wait_ge(opened, p + 1)
                        for k in range(2):
                            load_indices(sp, p, 0, k, idx_ready)
                            load(p, k, k)
                        with sp.Fori(1, NG // 2) as i:
                            for k in range(2):
                                g = i * 2 + k
                                c2 = (p * NG + g - 1) * 2
                                sp.wait_ge(hid_mm, c2)
                                sp.wait_ge(tw_ready, c2)
                                load(p, g, k)
                                sp.wait_ge(pre_ready, c2)
                                load_indices(sp, p, i, k, idx_ready)

                @block.gpsimd
                def _(pool):
                    pool.memset(carrier[:, :], 0.0).then_inc(carried, 1)
                    with pool.Fori(0, spans) as p:
                        with pool.Fori(0, NG // 2) as i:
                            for k in range(2):
                                gather(pool, p, i, k, table3, idx_ready, landed, carried)

                @block.tensor
                def _(pe):
                    with pe.Fori(0, spans) as p:
                        pe.wait_ge(opened, p + 1)

                        def step(s, n, k, local):
                            def within(c):
                                return s is None or 0 <= s + c < NC

                            if within(1):
                                q = (k + 1) % 4
                                if q % 2 == 0:
                                    pe.wait_ge(ea_ready[q // 2], (n + 1 - q) * 4 + 16)
                                if s is None or s + 1 >= 2:
                                    pe.wait_ge(hid_ready, n)
                                pe.matmul(banks[q % 2][:, :], we1_sb[:, :], ea[:, q // 2, (q % 2) * CE:(q % 2 + 1) * CE],
                                          start=True, stop=True).then_inc(hid_mm, 1)
                            if within(0):
                                pe.wait_ge(hid_ready, n + 1)
                                if s is None or s >= 2:
                                    pe.wait_ge(ef_ready, n - 1)
                                pe.matmul(banks[2 + k % 2][:, :], we2_sb[:, :], hid[:, k % 2, :],
                                          start=True, stop=True).then_inc(ef_mm, 1)
                            if within(-1):
                                b = (k - 1) % 2
                                pe.wait_ge(ef_ready, n)
                                if s is None or s - 1 >= 2:
                                    pe.wait_ge(pre_ready, n - 2)
                                for t in range(CH):
                                    last = pe.matmul(banks[4 + b][:, t * C:(t + 1) * C], ef[:, b, t * P:(t + 1) * P],
                                                     wn1b_sb[:, :], start=True, stop=True)
                                last.then_inc(pre_mm, 1)
                            if within(-2):
                                q = (k - 2) % 4
                                pe.wait_ge(msg_ready, n - 1)
                                if q % 2 == 0:
                                    pe.wait_ge(hot_of[q // 2], n - 2 - q + 4)
                                    if s is None or s - 2 >= 4:
                                        pe.wait_ge(added_of[q // 2], n - 2 - q)
                                for t in range(CH):
                                    last = pe.matmul(banks[6 + q // 2][:, 0:WIN], msg[:, q % 2, t * C:(t + 1) * C],
                                                     onehot[:, q // 2, (q % 2) * CH + t, 1, :],
                                                     start=(t == 0 and q % 2 == 0), stop=(t == CH - 1 and q % 2 == 1))
                                last.then_inc(seg_mm, 1)

                        steps(pe, p, step)

                @block.scalar
                def _(act):
                    with act.Fori(0, spans) as p:
                        act.wait_ge(opened, p + 1)

                        def step(s, n, k, local):
                            def within(c):
                                return s is None or 0 <= s + c < NC

                            if within(1):
                                q = (k + 1) % 4
                                act.wait_ge(hid_mm, n + 2)
                                if s is None or s + 1 >= 2:
                                    act.wait_ge(ef_mm, n)
                                act.activation(hid[:, q % 2, :], banks[q % 2][:, :], ACT.Relu,
                                               bias=be1_col[:, 0:1]).then_inc(hid_ready, 1)
                                if q % 2 == 0:
                                    act.wait_ge(ts_ready[q // 2], (n + 1 - q) * 4 + 16)
                                if s is None or s + 1 >= 2:
                                    act.wait_ge(ef_ready, n)
                                act.activation(tw[:, q % 2, :], tsb[:, q // 2, (q % 2) * CE:(q % 2 + 1) * CE], ACT.Sigmoid,
                                               bias=bt_col[:, 0:1], scale=wt_col[:, 0:1]).then_inc(tw_ready, 1)
                            if within(-1):
                                b = (k - 1) % 2
                                act.wait_ge(pre_ready, n)
                                if s is None or s - 1 >= 2:
                                    act.wait_ge(seg_mm, n - 2)
                                act.activation(msg[:, b, :], pre[:, b, :], ACT.Relu).then_inc(msg_ready, 1)

                        steps(act, p, step)

                @block.vector
                def _(dve):
                    dve.tensor_copy(lo_now[:, :], lo[:, :]).then_inc(own, 1)
                    with dve.Fori(0, spans) as p:
                        dve.wait_ge(own, p * 4 + 1)
                        open_pass(dve, p, 0, own)
                        dve.nop().then_inc(opened, 1)

                        def step(s, n, k, local):
                            def within(c):
                                return s is None or 0 <= s + c < NC

                            if within(0):
                                b = k % 2
                                dve.wait_ge(ef_mm, n + 1)
                                dve.wait_ge(tw_ready, n + 1)
                                if s is None or s >= 2:
                                    dve.wait_ge(pre_mm, n - 1)
                                dve.scalar_tensor_tensor(out=ef[:, b, :], in0=banks[2 + b][:, :], scalar=be2_col[:, 0:1],
                                                         in1=tw[:, b, :], op0=ALU.add, op1=ALU.mult).then_inc(ef_ready, 1)
                                if k % 2 == 0:
                                    if s is None or s >= 4:
                                        dve.wait_ge(seg_mm, n - 2)
                                    one_hot(dve, k // 2, (local - k) // 2 + k // 2, 1).then_inc(hot_of[k // 2], 4)
                            if within(-1):
                                q = (k - 1) % 4
                                b = q % 2
                                dve.wait_ge(pre_mm, n)
                                if s is None or s - 1 >= 2:
                                    dve.wait_ge(msg_ready, n - 2)
                                for t in range(CH):
                                    dve.wait_ge(landed[q // 2][(q % 2) * CH + t], (n - 1 - q) * 4 + 16)
                                rows_ = got[:, q // 2, (q % 2) * CH:(q % 2 + 1) * CH, :]
                                dve.tensor_tensor(pre[:, b, :].rearrange("q (t c) -> q t c", t=CH),
                                                  banks[4 + b][:, :].rearrange("q (t c) -> q t c", t=CH),
                                                  rows_, ALU.add).then_inc(pre_ready, 1)
                            if within(-3) and (k - 3) % 2 == 1:
                                q = (k - 3) % 4
                                add(q // 2, n - 3, (local - 3 - q) // 2 + q // 2, s is not None and s - 3 < 4)

                        def add(slot, n, g, first):
                            win = dve.value_load(win_i[0:1, bass.ds(g, 1)], min_val=0, max_val=LASTWIN)
                            dve.wait_ge(seg_mm, n + 1)
                            a = acc[:, bass.ds(win, WIN)]
                            if slot == 1 or not first:
                                dve.wait_ge(added_of[1 - slot], n + 1 if slot else n - 1)
                            dve.tensor_tensor(a, a, banks[6 + slot][:, 0:WIN], ALU.add).then_inc(added_of[slot], 4)

                        steps(dve, p, step)
                        add(1, p * NC + NC - 1, NG - 1, False)
                        dve.wait_ge(added_of[1], p * NC + NC)

        def final_stage():
            c = sem("out_chain")
            mm = sem("out_mm")
            summed = sem("out_summed")
            rooted = sem("out_rooted")
            stored = sem("out_stored")
            with nc.Block() as block:
                @block.tensor
                def _(pe):
                    for t in range(NT):
                        if t >= 8:
                            pe.wait_ge(summed, t - 7)
                        s = slice(t * NP, (t + 1) * NP)
                        b = banks[t % 8][0:NP, 0:C]
                        pe.matmul(b, acc[:, s], wn2_sb[:, :], start=True, stop=False)
                        pe.matmul(b, degcnt[0:1, 1, s], bn2_row[:, :], start=False, stop=True).then_inc(mm, 1)

                @block.vector
                def _(dve):
                    for t in range(NT):
                        dve.wait_ge(mm, t + 1)
                        dve.scalar_tensor_tensor(out=scr_rows[:, t, :], in0=x1_rows[:, t, :], scalar=2.0,
                                                 in1=banks[t % 8][0:NP, 0:C], op0=ALU.mult, op1=ALU.add).then_inc(summed, 1)
                    dve.wait_ge(summed, NT)
                    layer_norm(dve, x_rows, c, 0, rooted)

                @block.scalar
                def _(act):
                    act.wait_ge(c, NT + 1)
                    act.activation(sdev[:, :], mv[:, :, 1], ACT.Sqrt, bias=eps_col[0:NP, 0:1]).then_inc(rooted, 1)

                @block.sync
                def _(sp):
                    sp.wait_ge(c, NT + 3)
                    sp.dma_start(node_rows(out), x_rows[:, :, :]).then_inc(stored, 16)
                    sp.wait_ge(stored, 16)

        hot_of = [sem(f"msg_hot{k}") for k in range(2)]
        added_of = [sem(f"msg_added{k}") for k in range(2)]
        degree_stage()
        scale_stage()
        conv_stage("conv1", table1)
        hidden_stage()
        conv_stage("conv2", table2)
        middle_stage()
        message_stage()
        final_stage()


def kernel(x, src, dst, edge_attr_64, edge_weight, L0_gnn_W1, L0_gnn_b1, L0_gnn_W2, L0_gnn_b2,
           L1_gnn_We1, L1_gnn_be1, L1_gnn_We2, L1_gnn_be2, L1_gnn_Wt, L1_gnn_bt,
           L1_gnn_Wn1, L1_gnn_bn1, L1_gnn_Wn2, L1_gnn_bn2):
    import numpy as np
    import concourse.bacc as bacc
    from concourse.bass_utils import run_bass_kernel_spmd

    def padded(a, value, rows):
        a = np.asarray(a)
        return np.concatenate([a, np.full((rows - a.shape[0],) + a.shape[1:], value, a.dtype)])

    def by_tile(a, value):
        return np.ascontiguousarray(padded(a, value, EP).reshape(TILES, P).T)

    arrays = {
        "x": np.ascontiguousarray(x), "xt": np.ascontiguousarray(np.asarray(x).T),
        "src": by_tile(src, 0).view(np.uint32), "dst": by_tile(dst, N), "ew": by_tile(edge_weight, 0),
        "ew_row": padded(edge_weight, 0, EP).reshape(1, EP),
        "ea_t": np.ascontiguousarray(padded(edge_attr_64, 0, EP).T),
        "w1": L0_gnn_W1, "b1": L0_gnn_b1, "w2": L0_gnn_W2, "b2": L0_gnn_b2,
        "we1": L1_gnn_We1, "be1": L1_gnn_be1, "we2": L1_gnn_We2, "be2": L1_gnn_be2,
        "wt": L1_gnn_Wt, "bt": L1_gnn_bt, "wn1": L1_gnn_Wn1, "bn1": L1_gnn_bn1,
        "wn2": L1_gnn_Wn2, "bn2": L1_gnn_bn2,
    }
    arrays = {k: np.asarray(v) for k, v in arrays.items()}
    nc = bacc.Bacc("TRN2", target_bir_lowering=False, num_devices=1)
    aps = {k: nc.dram_tensor("in_" + k, v.shape, mybir.dt.from_np(v.dtype), kind="ExternalInput").ap()
           for k, v in arrays.items()}
    out = nc.dram_tensor("out_x", (N, C), F32, kind="ExternalOutput").ap()
    build(nc, out=out, **aps)
    r = run_bass_kernel_spmd(nc, [{"in_" + k: v for k, v in arrays.items()}], core_ids=[0])
    return r.results[0]["out_x"]
```
